# Optimizing a Trainium2 kernel written in Bass

```python
import numpy as np
import jax
import jax.numpy as jnp

def _softmax(x, axis=-1):
    return jax.nn.softmax(x, axis=axis)

def _gelu(x):
    return jax.nn.gelu(x, approximate=True)

def _silu(x):
    return jax.nn.silu(x)

def _sigmoid(x):
    return jax.nn.sigmoid(x)

def _layernorm(x, axis=-1, eps=1e-05):
    m = jnp.mean(x, axis=axis, keepdims=True)
    v = jnp.var(x, axis=axis, keepdims=True)
    return (x - m) / jnp.sqrt(v + eps)

def _scatter_add(tgt, idx, src, axis=0):
    return tgt.at[idx].add(src)

def _segment_sum(src, seg, n):
    return jax.ops.segment_sum(src, seg, n)
kernel_name = 'mk_adaln_ffn_d1_seqx_r8_69b75e'

def setup_inputs(seed: int=0):
    np.random.seed(seed)
    _w = jnp.asarray

    def _rec_inputs():
        import jax
        import jax.numpy as jnp
        _rk = jax.random.key(seed)
        x = -0.000125 + 0.9999 * jax.random.normal(jax.random.fold_in(_rk, 1), (128, 32, 512), jnp.float32)
        _lenS = 32 - jax.random.randint(jax.random.fold_in(_rk, 7), (128,), 0, max(1, 32 // 4) + 1, jnp.int32)
        _lenS2 = 32 - jax.random.randint(jax.random.fold_in(_rk, 8), (128,), 0, max(1, 32 // 4) + 1, jnp.int32)
        itok_B_0_7 = jax.random.randint(jax.random.fold_in(_rk, 11), (128,), 0, 8, jnp.int32)
        return (x, itok_B_0_7)
    x, itok_B_0_7 = _rec_inputs()

    def _L0_cond_setup():
        import jax, jax.numpy as jnp
        import numpy as np
        TOP_K = 2
        LANG_BIAS = 5.0
        SCALING = 32.0 / 16.0
        LANGUAGE_PAD_ID = -1
        key = jax.random.key(seed)
        ks = jax.random.split(key, 6)
        B, T, D, O, E, R = (4, 256, 512, 512, 8, 16)
        x = jax.random.normal(ks[0], (B, T, D), dtype=jnp.float32)
        language_ids = jax.random.randint(ks[1], (B,), 0, E).astype(jnp.int64)
        W = jax.random.normal(ks[2], (O, D), dtype=jnp.float32) * (1.0 / np.sqrt(D))
        Wr = jax.random.normal(ks[3], (E, D), dtype=jnp.float32) * (1.0 / np.sqrt(D))
        A = jax.random.normal(ks[4], (E, R, D), dtype=jnp.float32) * (1.0 / np.sqrt(D))
        Bm = jax.random.normal(ks[5], (O, R), dtype=jnp.float32) * 0.0
        Bm = jnp.broadcast_to(Bm, (E, O, R)) + jax.random.normal(ks[5], (E, O, R), dtype=jnp.float32) * 0.02
        return {'x': x, 'language_ids': language_ids, 'W': W, 'Wr': Wr, 'A': A, 'B': Bm}
    _L0_cond_all = _L0_cond_setup()
    _L0_cond_in = {k: v for k, v in _L0_cond_all.items() if k in ('W', 'Wr', 'A', 'B')}
    del _L0_cond_all

    def _L0_ffn_setup():
        import jax, jax.numpy as jnp
        import numpy as np
        D_IN, D_OUT = (512, 512)
        B, S = (2, 256)
        key = jax.random.key(seed)
        kx, kw = jax.random.split(key)
        x = jax.random.normal(kx, (B, S, D_IN), dtype=jnp.float32)
        w = jax.random.normal(kw, (D_IN, D_OUT), dtype=jnp.float32)
        sign = jnp.where(w >= 0, 1.0, -1.0).astype(jnp.float32)
        scale = jnp.abs(w).mean().astype(jnp.float32)
        return {'x': x, 'sign': sign, 'scale': scale}
    _L0_ffn_all = _L0_ffn_setup()
    _L0_ffn_in = {k: v for k, v in _L0_ffn_all.items() if k in ('sign', 'scale')}
    del _L0_ffn_all
    return {'x': x, 'itok_B_0_7': itok_B_0_7, 'L0_cond_W': _L0_cond_in['W'], 'L0_cond_Wr': _L0_cond_in['Wr'], 'L0_cond_A': _L0_cond_in['A'], 'L0_cond_B': _L0_cond_in['B'], 'L0_ffn_sign': _L0_ffn_in['sign'], 'L0_ffn_scale': _L0_ffn_in['scale']}

def reference(x, itok_B_0_7, L0_cond_W, L0_cond_Wr, L0_cond_A, L0_cond_B, L0_ffn_sign, L0_ffn_scale):
    import jax
    import jax.numpy as jnp

    def _L0_cond_ref(x, language_ids, W, Wr, A, B):
        import jax, jax.numpy as jnp
        import numpy as np
        TOP_K = 2
        LANG_BIAS = 5.0
        SCALING = 32.0 / 16.0
        LANGUAGE_PAD_ID = -1
        base = jnp.einsum('btd,od->bto', x, W)
        E = Wr.shape[0]
        logits = jnp.einsum('btd,ed->bte', x.astype(jnp.float32), Wr.astype(jnp.float32))
        expert_targets = language_ids
        valid = expert_targets >= 0
        tgt = jnp.where(valid, expert_targets, 0)
        bias = jax.nn.one_hot(tgt, E, dtype=logits.dtype) * LANG_BIAS
        bias = jnp.where(valid[:, None], bias, 0.0)
        logits = logits + bias[:, None, :]
        topw, topi = jax.lax.top_k(logits, TOP_K)
        weights = jax.nn.softmax(topw, axis=-1)
        gates = jnp.sum(jax.nn.one_hot(topi, E, dtype=weights.dtype) * weights[..., None], axis=-2)
        gates = gates.astype(x.dtype)
        h = jnp.einsum('btd,erd->bter', x, A)
        lora_out = jnp.einsum('bter,bte,eor->bto', h, gates, B)
        return base + SCALING * lora_out

    def _L0_ffn_ref(x, sign, scale):
        import jax, jax.numpy as jnp
        import numpy as np
        D_IN, D_OUT = (512, 512)
        B, S = (2, 256)
        s = jax.nn.softplus(scale)
        return jnp.einsum('bsi,io->bso', x, sign) * s
    x = x + _L0_ffn_ref(_L0_cond_ref(x, itok_B_0_7, L0_cond_W, L0_cond_Wr, L0_cond_A, L0_cond_B), L0_ffn_sign, L0_ffn_scale)
    return x

_drawn_inputs = setup_inputs


def setup_inputs(seed=0):
    import zlib

    import numpy as np

    out = dict(_drawn_inputs(seed))
    spreads = {}
    factors = {'L0_cond_Wr': 3.679}
    for name, (base, spread) in spreads.items():
        noise = np.random.default_rng([zlib.crc32(name.encode()), seed]).standard_normal(out[name].shape)
        drawn = base * np.exp(spread * noise) if base else spread * noise
        out[name] = jnp.asarray(drawn.astype(out[name].dtype))
    for name, factor in factors.items():
        out[name] = (out[name] * factor).astype(out[name].dtype)
    return out
```

```python
import concourse.bass as bass
from concourse import mybir
from contextlib import ExitStack

FP32 = mybir.dt.float32
FP32R = mybir.dt.float32r
INT32 = mybir.dt.int32
UINT32 = mybir.dt.uint32
ALU = mybir.AluOpType
ACT = mybir.ActivationFunctionType

P = 128
Q = 32
LANG_BIAS = 5.0
SCALING = 32.0 / 16.0


def adaln_ffn_kernel(nc: bass.Bass, x, lang_ids, W, Wr, A, B, sign, scale, out):
    BATCH, TILES, D = x.shape
    O = W.shape[0]
    E, R = A.shape[0], A.shape[1]
    ER = E * R
    NQ = P // Q
    KC = D // P
    OC = O // P
    HEAD = E + ER
    WIDE = HEAD + D
    HALF = WIDE // 2
    Y0 = HALF - HEAD
    assert BATCH == P and ER == P and D % (NQ * Q) == 0 and WIDE % 2 == 0 and O == KC * P
    S3 = 3

    x_load = x.rearrange("(g b) t (i c) -> i b t g c", b=Q, i=NQ)
    w_load = W.rearrange("(p j) d -> p j d", j=OC)
    sign_load = sign.rearrange("(p j) n -> p j n", j=OC)
    a_load = A.rearrange("e r d -> (e r) d").rearrange("(g b) (i c) -> i b g c", b=Q, i=NQ)
    wr_load = Wr.rearrange("e (i c) -> i e c", i=NQ)
    b_load = B.rearrange("e (p j) r -> p e (j r)", j=OC)

    ctx = ExitStack()
    with ctx:
        def sb(name, shape, dt=FP32):
            return ctx.enter_context(nc.sbuf_tensor(name, shape, dt))

        def sem(name):
            return ctx.enter_context(nc.semaphore(name))

        w_in = sb("w_in", [P, OC, D])
        sign_in = sb("sign_in", [P, OC, D])
        a_in = sb("a_in", [P, NQ, P])
        wr_in = sb("wr_in", [P, P])
        at = sb("at", [P, NQ, KC, Q])
        wrt = sb("wrt", [P, KC, Q])
        b_in = sb("b_in", [P, E, OC * R])
        ids_in = sb("ids_in", [P, 1], INT32)
        scale_in = sb("scale_in", [P, 1])
        w_hi = sb("w_hi", [P, OC, KC, NQ, Q], FP32R)
        w_lo = sb("w_lo", [P, OC, KC, NQ, Q], FP32R)
        sign_hi = sb("sign_hi", [P, OC, D], FP32R)
        sign_lo = sb("sign_lo", [P, OC, D], FP32R)
        b_hi = sb("b_hi", [P, OC, E, R], FP32R)
        b_lo = sb("b_lo", [P, OC, E, R], FP32R)
        wide_hi = sb("wide_hi", [P, KC, WIDE], FP32R)
        wide_lo = sb("wide_lo", [P, KC, WIDE], FP32R)
        m_full = sb("m_full", [P, KC, D])
        b2_hi = sb("b2_hi", [P, D], FP32R)
        b2_lo = sb("b2_lo", [P, D], FP32R)
        ident = sb("ident", [P, P])
        eye = sb("eye", [P, KC, D])
        expert_no_int = sb("expert_no_int", [P, E], INT32)
        expert_no = sb("expert_no", [P, E])
        lang = sb("lang", [P, 1])
        bias = sb("bias", [P, E])
        sp = sb("sp", [P, 12])
        exp_neg = sb("exp_neg", [P, 1])
        ln_one = sb("ln_one", [P, 1])
        x_in = [sb(f"x_in{n}", [P, NQ, P]) for n in range(S3)]
        xt = [sb(f"xt{n}", [P, NQ, KC, Q]) for n in range(S3)]
        xt_hi = [sb(f"xt_hi{n}", [P, KC, P], FP32R) for n in range(S3)]
        xt_lo = [sb(f"xt_lo{n}", [P, KC, P], FP32R) for n in range(S3)]
        logits = sb("logits", [P, E])
        top = sb("top", [P, 8])
        top_at = sb("top_at", [P, 8], UINT32)
        top_no = sb("top_no", [P, 2])
        e2 = sb("e2", [P, 1])
        denom = sb("denom", [P, 1])
        rdenom = sb("rdenom", [P, 1])
        second = sb("second", [P, E])
        gate = sb("gate", [P, E])
        h_gated = sb("h_gated", [P, ER])
        ht_hi = sb("ht_hi", [ER, P], FP32R)
        ht_lo = sb("ht_lo", [ER, P], FP32R)
        y = [sb(f"y{n}", [P, D]) for n in range(S3)]

        pair = [[ctx.enter_context(nc.psum_tensor(f"pair{n}{k}", [P, 512], FP32)) for k in range(2)]
                for n in range(S3)]
        p_ht = ctx.enter_context(nc.psum_tensor("p_ht", [P, 512], FP32))
        p_b2 = ctx.enter_context(nc.psum_tensor("p_b2", [P, 512], FP32))
        p_m = [pair[1][0], pair[1][1], pair[2][0], pair[2][1]]

        a_loaded = sem("a_loaded")
        wr_loaded = sem("wr_loaded")
        w_loaded = [sem(f"w_loaded{j}") for j in range(OC)]
        sign_loaded = [sem(f"sign_loaded{j}") for j in range(OC)]
        b_loaded = sem("b_loaded")
        scale_loaded = sem("scale_loaded")
        ids_loaded = sem("ids_loaded")
        zeroed = sem("zeroed")
        ident_made = sem("ident_made")
        eye_made = sem("eye_made")
        experts_numbered = sem("experts_numbered")
        vec_done = sem("vec_done")
        bias_made = sem("bias_made")
        exp_neg_made = sem("exp_neg_made")
        neg_abs_made = sem("neg_abs_made")
        ln_one_made = sem("ln_one_made")
        softplus_made = sem("softplus_made")
        wr_zeroed = sem("wr_zeroed")
        head_turned = sem("head_turned")
        head_hi_made = sem("head_hi_made")
        head_lo_made = sem("head_lo_made")
        w_hi_made = sem("w_hi_made")
        sign_hi_made = sem("sign_hi_made")
        ws_lo_made = sem("ws_lo_made")
        b_hi_made = sem("b_hi_made")
        b_lo_made = sem("b_lo_made")
        m_summed = sem("m_summed")
        m_full_made = sem("m_full_made")
        m_hi_made = sem("m_hi_made")
        m_lo_made = sem("m_lo_made")
        b2_summed = sem("b2_summed")
        b2_hi_made = sem("b2_hi_made")
        b2_lo_made = sem("b2_lo_made")
        x_loaded = [sem(f"x_loaded{n}") for n in range(S3)]
        y_stored = [sem(f"y_stored{n}") for n in range(S3)]
        xt_made = sem("xt_made")
        xt_hi_made = sem("xt_hi_made")
        xt_lo_made = sem("xt_lo_made")
        head_ready = sem("head_ready")
        wide_done = sem("wide_done")
        logits_made = sem("logits_made")
        top_made = sem("top_made")
        top_at_made = sem("top_at_made")
        top_no_made = sem("top_no_made")
        e2_made = sem("e2_made")
        denom_made = sem("denom_made")
        rdenom_made = sem("rdenom_made")
        second_made = sem("second_made")
        gate_made = sem("gate_made")
        h_gated_made = sem("h_gated_made")
        ht_turned = sem("ht_turned")
        ht_hi_made = sem("ht_hi_made")
        ht_lo_made = sem("ht_lo_made")
        y_summed = sem("y_summed")
        y_copied = sem("y_copied")

        block = ctx.enter_context(nc.Block())

        def slot(r, d=0):
            return (r + d) % S3

        def turn(q, r, d=0):
            return q + (r + d) // S3

        LEAD = 2
        LAG = 2
        FIRST = LAG + S3
        LOOPS = (TILES - LEAD - FIRST) // S3
        AFTER = FIRST + S3 * LOOPS

        def steps(eng, step):
            for s in range(FIRST):
                step(s // S3, s % S3, s)
            with eng.Fori(1, 1 + LOOPS) as q:
                for r in range(FIRST - S3, FIRST):
                    step(q, r, None)
            for s in range(AFTER, TILES + LAG):
                step(s // S3, s % S3, s)

        def has(s, d):
            return s is None or 0 <= s + d < TILES

        @block.sync
        def _(sp_eng):
            def load(q, r, t):
                for i in range(NQ):
                    sp_eng.dma_start(x_in[r % S3][Q * i:Q * i + Q, :, :], x_load[i, :, t, :, :])\
                        .then_inc(x_loaded[r % S3], 16)

            def store(q, r, d):
                sp_eng.wait_ge(y_copied, S3 * q + r + d + 1)
                sp_eng.dma_start(out[:, S3 * q + r + d, :], y[slot(r, d)][:, :])\
                    .then_inc(y_stored[slot(r, d)], 16)

            for i in range(NQ):
                sp_eng.dma_start(a_in[Q * i:Q * i + Q, :, :], a_load[i, :, :, :]).then_inc(a_loaded, 16)
            sp_eng.wait_ge(wr_zeroed, 1)
            for i in range(NQ):
                sp_eng.dma_start(wr_in[Q * i:Q * i + E, :], wr_load[i, :, :]).then_inc(wr_loaded, 16)
            for j in range(OC):
                sp_eng.dma_start(w_in[:, j, :], w_load[:, j, :]).then_inc(w_loaded[j], 16)
                sp_eng.dma_start(sign_in[:, j, :], sign_load[:, j, :]).then_inc(sign_loaded[j], 16)
            sp_eng.dma_start(b_in[:, :, :], b_load).then_inc(b_loaded, 16)
            for t in range(S3):
                load(0, t, t)

            def turnover(q, r, s):
                if s is None or s + S3 < TILES:
                    sp_eng.wait_ge(xt_made, S3 * q + r + 1)
                    load(q, r, S3 * q + r + S3)
                if s is None or s >= LAG + LEAD:
                    store(q, r, -LAG - LEAD)

            for s in range(LAG + LEAD):
                turnover(s // S3, s % S3, s)
            loops = (TILES - S3 - LAG - LEAD) // S3
            with sp_eng.Fori(1, 1 + loops) as q:
                for r in range(LAG + LEAD - S3, LAG + LEAD):
                    turnover(q, r, None)
            for s in range(LAG + LEAD + S3 * loops, TILES + LAG + LEAD):
                turnover(s // S3, s % S3, s)
            for n in range(S3):
                sp_eng.wait_ge(y_stored[n], 16 * len(range(n, TILES, S3)))

        @block.gpsimd
        def _(pool):
            nc.gpsimd.memset(wr_in[:, :], 0.0).then_inc(wr_zeroed, 1)
            nc.gpsimd.iota(expert_no_int[:, :], [[1, E]], base=0, channel_multiplier=0)\
                .then_inc(experts_numbered, 1)
            nc.gpsimd.memset(ident[:, :], 0.0).then_inc(zeroed, 1)
            pool.wait_ge(zeroed, 1)
            nc.gpsimd.affine_select(out=ident[:, :], in_=ident[:, :], compare_op=ALU.not_equal, fill=1.0,
                                    base=0, pattern=[[-1, P]], channel_multiplier=1).then_inc(ident_made, 1)
            nc.gpsimd.memset(eye[:, :, :], 0.0).then_inc(zeroed, 1)
            pool.wait_ge(zeroed, 2)
            for j in range(KC):
                part = eye[:, j, :].rearrange("p (i k a) -> p i k a", i=NQ, k=KC)[:, :, j, :]
                nc.gpsimd.affine_select(out=part, in_=part, compare_op=ALU.not_equal, fill=1.0, base=0,
                                        pattern=[[-Q, NQ], [-1, Q]], channel_multiplier=1)\
                    .then_inc(eye_made, 1)

            def low_x(q, r, d):
                pool.wait_ge(xt_hi_made, S3 * q + r + d + 1)
                n = slot(r, d)
                nc.gpsimd.tensor_tensor(xt_lo[n][:, :, :].rearrange("p j (g b) -> p g j b", g=NQ),
                                        xt[n][:, :, :, :],
                                        xt_hi[n][:, :, :].bitcast(FP32).rearrange("p j (g b) -> p g j b", g=NQ),
                                        ALU.subtract).then_inc(xt_lo_made, 1)

            for t in range(LEAD):
                low_x(0, t, 0)

            def step(q, r, s):
                if has(s, LEAD):
                    low_x(q, r, LEAD)

            steps(pool, step)

        @block.scalar
        def _(act):
            act.dma_start(scale_in[:, :], scale.partition_broadcast(P)).then_inc(scale_loaded, 16)
            act.dma_start(ids_in[:, :], lang_ids.rearrange("(p a) -> p a", a=1)).then_inc(ids_loaded, 16)
            act.wait_ge(neg_abs_made, 1)
            nc.scalar.activation(exp_neg[:, :], sp[:, 1:2], ACT.Exp).then_inc(exp_neg_made, 1)
            act.wait_ge(exp_neg_made, 1)
            nc.scalar.activation(ln_one[:, :], exp_neg[:, :], ACT.Ln, bias=1.0).then_inc(ln_one_made, 1)
            act.wait_ge(head_turned, 2)
            nc.scalar.activation(wide_hi[:, :, 0:E], wrt[:, :, 0:E], ACT.Copy).then_inc(head_hi_made, 1)
            nc.scalar.activation(wide_hi[:, :, E:HEAD].rearrange("p j (g b) -> p g j b", g=NQ), at[:, :, :, :],
                                 ACT.Copy).then_inc(head_hi_made, 1)
            for j in range(OC):
                act.wait_ge(w_loaded[j], 16)
                nc.scalar.activation(w_hi[:, j, :, :, :],
                                     w_in[:, j, :].rearrange("p (i k a) -> p k i a", i=NQ, k=KC),
                                     ACT.Copy).then_inc(w_hi_made, 1)
                act.wait_ge(sign_loaded[j], 16)
                nc.scalar.activation(sign_hi[:, j, :], sign_in[:, j, :], ACT.Copy).then_inc(sign_hi_made, 1)
            act.wait_ge(b_loaded, 16)
            nc.scalar.activation(b_hi[:, :, :, :], b_in[:, :, :].rearrange("p e (j r) -> p j e r", j=OC),
                                 ACT.Copy).then_inc(b_hi_made, 1)

            def high_x(q, r, d, first=False):
                n = slot(r, d)
                act.wait_ge(xt_made, S3 * q + r + d + 1)
                if not first:
                    act.wait_ge(wide_done, S3 * q + r + d + 1 - S3)
                nc.scalar.activation(xt_hi[n][:, :, :].rearrange("p j (g b) -> p g j b", g=NQ),
                                     xt[n][:, :, :, :], ACT.Copy).then_inc(xt_hi_made, 1)

            for t in range(LEAD):
                high_x(0, t, 0, first=True)
            for k in range(KC):
                act.wait_ge(m_full_made, k + 1)
                nc.scalar.activation(wide_hi[:, k, HEAD:WIDE], m_full[:, k, :], ACT.Copy).then_inc(m_hi_made, 1)
            act.wait_ge(b2_summed, 1)
            nc.scalar.activation(b2_hi[:, :], p_b2[:, :], ACT.Copy, scale=sp[:, 11:12]).then_inc(b2_hi_made, 1)

            def step(q, r, s):
                if has(s, -LAG):
                    act.wait_ge(ht_turned, S3 * q + r - LAG + 1)
                    nc.scalar.activation(ht_hi[:, :], p_ht[:, 0:P], ACT.Copy).then_inc(ht_hi_made, 1)
                if has(s, -1):
                    act.wait_ge(top_made, S3 * q + r)
                    nc.scalar.activation(e2[:, :], top[:, 0:1], ACT.Exp, bias=top[:, 1:2], scale=-1.0)\
                        .then_inc(e2_made, 1)
                if has(s, -LAG):
                    n = slot(r, -LAG)
                    act.wait_ge(y_summed, S3 * q + r - LAG + 1)
                    if s is None or s - LAG >= S3:
                        act.wait_ge(y_stored[n], 16 * turn(q, r, -LAG))
                    nc.scalar.activation(y[n][:, 0:Y0], pair[n][0][:, HEAD:HALF], ACT.Copy)
                    nc.scalar.activation(y[n][:, Y0:D], pair[n][1][:, 0:HALF], ACT.Copy).then_inc(y_copied, 1)
                if has(s, LEAD):
                    high_x(q, r, LEAD, first=(s is not None and s + LEAD < S3))

            steps(act, step)

        @block.vector
        def _(dve):
            chain = [0]

            def link(ins):
                chain[0] += 1
                ins.then_inc(vec_done, 1)
                dve.wait_ge(vec_done, chain[0])

            dve.wait_ge(wr_loaded, 16 * NQ)
            nc.vector.transpose(wrt[:, :, :].rearrange("p j b -> p (j b)"), wr_in[:, :]).then_inc(head_turned, 1)
            dve.wait_ge(a_loaded, 16 * NQ)
            nc.vector.transpose(at[:, :, :, :].rearrange("p g j b -> p (g j b)"),
                                a_in[:, :, :].rearrange("p g c -> p (g c)")).then_inc(head_turned, 1)
            dve.wait_ge(scale_loaded, 16)
            link(nc.vector.tensor_scalar(sp[:, 0:1], scale_in[:, :], -1.0, None, ALU.mult))
            nc.vector.tensor_tensor(sp[:, 1:2], sp[:, 0:1], scale_in[:, :], ALU.min).then_inc(neg_abs_made, 1)
            dve.wait_ge(ids_loaded, 16)
            dve.wait_ge(experts_numbered, 1)
            nc.vector.tensor_copy(expert_no[:, :], expert_no_int[:, :])
            link(nc.vector.tensor_copy(lang[:, :], ids_in[:, :]))
            nc.vector.tensor_scalar(bias[:, :], expert_no[:, :], lang[:, 0:1], LANG_BIAS, ALU.is_equal, ALU.mult)\
                .then_inc(bias_made, 1)
            dve.wait_ge(exp_neg_made, 1)
            link(nc.vector.tensor_scalar(sp[:, 2:3], exp_neg[:, :], 1.0, None, ALU.add))
            link(nc.vector.tensor_scalar(sp[:, 3:4], sp[:, 2:3], -1.0, None, ALU.add))
            link(nc.vector.tensor_scalar(sp[:, 4:5], sp[:, 3:4], 0.0, None, ALU.is_equal))
            link(nc.vector.tensor_tensor(sp[:, 5:6], sp[:, 3:4], sp[:, 4:5], ALU.add))
            link(nc.vector.reciprocal(sp[:, 6:7], sp[:, 5:6]))
            dve.wait_ge(ln_one_made, 1)
            link(nc.vector.tensor_tensor(sp[:, 7:8], ln_one[:, :], sp[:, 4:5], ALU.add))
            link(nc.vector.tensor_tensor(sp[:, 8:9], sp[:, 7:8], sp[:, 6:7], ALU.mult))
            link(nc.vector.tensor_tensor(sp[:, 9:10], sp[:, 8:9], exp_neg[:, :], ALU.mult))
            link(nc.vector.scalar_tensor_tensor(sp[:, 10:11], scale_in[:, :], 0.0, sp[:, 9:10], ALU.max, ALU.add))
            nc.vector.tensor_scalar(sp[:, 11:12], sp[:, 10:11], SCALING, None, ALU.mult).then_inc(softplus_made, 1)
            softplus = sp[:, 10:11]

            dve.wait_ge(head_hi_made, 2)
            nc.vector.tensor_tensor(wide_lo[:, :, 0:E], wrt[:, :, 0:E], wide_hi[:, :, 0:E].bitcast(FP32),
                                    ALU.subtract)
            nc.vector.tensor_tensor(wide_lo[:, :, E:HEAD].rearrange("p j (g b) -> p g j b", g=NQ), at[:, :, :, :],
                                    wide_hi[:, :, E:HEAD].bitcast(FP32).rearrange("p j (g b) -> p g j b", g=NQ),
                                    ALU.subtract).then_inc(head_lo_made, 1)
            for j in range(OC):
                dve.wait_ge(w_hi_made, j + 1)
                nc.vector.tensor_tensor(w_lo[:, j, :, :, :],
                                        w_in[:, j, :].rearrange("p (i k a) -> p k i a", i=NQ, k=KC),
                                        w_hi[:, j, :, :, :].bitcast(FP32), ALU.subtract)
                dve.wait_ge(sign_hi_made, j + 1)
                nc.vector.tensor_tensor(sign_lo[:, j, :], sign_in[:, j, :], sign_hi[:, j, :].bitcast(FP32),
                                        ALU.subtract).then_inc(ws_lo_made, 1)

            dve.wait_ge(b_hi_made, 1)
            nc.vector.tensor_tensor(b_lo[:, :, :, :], b_in[:, :, :].rearrange("p e (j r) -> p j e r", j=OC),
                                    b_hi[:, :, :, :].bitcast(FP32), ALU.subtract).then_inc(b_lo_made, 1)

            def turn_x(q, r, d, first=False):
                n = slot(r, d)
                dve.wait_ge(x_loaded[n], 16 * NQ * (turn(q, r, d) + 1))
                if not first:
                    dve.wait_ge(xt_lo_made, S3 * q + r + d + 1 - S3)
                nc.vector.transpose(xt[n][:, :, :, :].rearrange("p g j b -> p (g j b)"),
                                    x_in[n][:, :, :].rearrange("p g c -> p (g c)")).then_inc(xt_made, 1)

            for t in range(LEAD):
                turn_x(0, t, 0, first=True)
            for k in range(KC):
                dve.wait_ge(m_summed, k + 1)
                dve.wait_ge(eye_made, KC)
                nc.vector.scalar_tensor_tensor(m_full[:, k, :], p_m[k][:, :], softplus, eye[:, k, :],
                                               ALU.mult, ALU.add).then_inc(m_full_made, 1)
                dve.wait_ge(m_hi_made, k + 1)
                nc.vector.tensor_tensor(wide_lo[:, k, HEAD:WIDE], m_full[:, k, :],
                                        wide_hi[:, k, HEAD:WIDE].bitcast(FP32),
                                        ALU.subtract).then_inc(m_lo_made, 1)
            dve.wait_ge(b2_hi_made, 1)
            nc.vector.scalar_tensor_tensor(b2_lo[:, :], p_b2[:, :], sp[:, 11:12], b2_hi[:, :].bitcast(FP32),
                                           ALU.mult, ALU.subtract).then_inc(b2_lo_made, 1)

            def step(q, r, s):
                done = S3 * q + r
                n = slot(r, -1)
                if has(s, -1):
                    dve.wait_ge(head_ready, done)
                    nc.vector.tensor_tensor(logits[:, :], pair[n][0][:, 0:E], bias[:, :], ALU.add)\
                        .then_inc(logits_made, 1)
                    dve.wait_ge(logits_made, done)
                if has(s, -LAG):
                    dve.wait_ge(ht_hi_made, done - LAG + 1)
                    nc.vector.tensor_tensor(ht_lo[:, :], p_ht[:, 0:P], ht_hi[:, :].bitcast(FP32), ALU.subtract)\
                        .then_inc(ht_lo_made, 1)
                if has(s, -1):
                    nc.vector.max(top[:, :], logits[:, :]).then_inc(top_made, 1)
                    dve.wait_ge(top_made, done)
                if has(s, LEAD):
                    turn_x(q, r, LEAD, first=(s is not None and s + LEAD < S3))
                if has(s, -1):
                    nc.vector.max_index(top_at[:, :], top[:, :], logits[:, :]).then_inc(top_at_made, 1)
                if has(s, -1):
                    dve.wait_ge(top_at_made, done)
                    nc.vector.tensor_copy(top_no[:, :], top_at[:, 0:2]).then_inc(top_no_made, 1)
                    dve.wait_ge(e2_made, done)
                    nc.vector.tensor_scalar(denom[:, :], e2[:, :], 1.0, None, ALU.add).then_inc(denom_made, 1)
                    dve.wait_ge(top_no_made, done)
                    nc.vector.tensor_scalar(second[:, :], expert_no[:, :], top_no[:, 1:2], e2[:, 0:1],
                                            ALU.is_equal, ALU.mult).then_inc(second_made, 1)
                    dve.wait_ge(denom_made, done)
                    nc.vector.reciprocal(rdenom[:, :], denom[:, :]).then_inc(rdenom_made, 1)
                    dve.wait_ge(second_made, done)
                    nc.vector.scalar_tensor_tensor(gate[:, :], expert_no[:, :], top_no[:, 0:1], second[:, :],
                                                   ALU.is_equal, ALU.add).then_inc(gate_made, 1)
                    dve.wait_ge(rdenom_made, done)
                    dve.wait_ge(gate_made, done)
                    nc.vector.scalar_tensor_tensor(
                        h_gated[:, :].rearrange("p (e r) -> p e r", e=E),
                        pair[n][0][:, E:HEAD].rearrange("p (e r) -> p e r", e=E), rdenom[:, 0:1],
                        gate[:, :].unsqueeze(2).to_broadcast([P, E, R]), ALU.mult, ALU.mult)\
                        .then_inc(h_gated_made, 1)

            steps(dve, step)

        @block.tensor
        def _(pe):
            pe.wait_ge(ident_made, 1)

            def three(out_ap, l_hi, l_lo, r_hi, r_lo, start, stop):
                nc.tensor.matmul(out_ap, l_hi, r_hi, start=start, stop=False, skip_group_check=True)
                nc.tensor.matmul(out_ap, l_hi, r_lo, start=False, stop=False, skip_group_check=True)
                return nc.tensor.matmul(out_ap, l_lo, r_hi, start=False, stop=stop, skip_group_check=True)

            for j in range(OC):
                pe.wait_ge(ws_lo_made, j + 1)
                for k in range(KC):
                    last = three(p_m[k][:, :], w_hi[:, j, k, :, :].rearrange("p i a -> p (i a)"),
                                 w_lo[:, j, k, :, :].rearrange("p i a -> p (i a)"),
                                 sign_hi[:, j, :], sign_lo[:, j, :], j == 0, j == OC - 1)
                    if j == OC - 1:
                        last.then_inc(m_summed, 1)
            pe.wait_ge(b_lo_made, 1)
            pe.wait_ge(head_lo_made, 1)
            for j in range(OC):
                last = three(p_b2[:, :], b_hi[:, j, :, :].rearrange("p e r -> p (e r)"),
                             b_lo[:, j, :, :].rearrange("p e r -> p (e r)"),
                             sign_hi[:, j, :], sign_lo[:, j, :], j == 0, j == OC - 1)
            last.then_inc(b2_summed, 1)

            def step(q, r, s):
                done = S3 * q + r

                def wide(chunks):
                    n = slot(r)
                    for k in chunks:
                        if s == 0:
                            pe.wait_ge(m_lo_made, k + 1)
                        for l, parts in ((xt_hi[n], (wide_hi, wide_lo)), (xt_lo[n], (wide_hi,))):
                            for w in parts:
                                start = k == 0 and l is xt_hi[n] and w is wide_hi
                                for half in range(2):
                                    last[half] = nc.tensor.matmul(
                                        pair[n][half][:, 0:HALF], l[:, k, :],
                                        w[:, k, HALF * half:HALF * half + HALF],
                                        start=start, stop=False, skip_group_check=True)

                last = [None, None]
                if has(s, 0):
                    pe.wait_ge(xt_lo_made, done + 1)
                    if s is None or s >= S3:
                        pe.wait_ge(y_copied, done - S3 + 1)
                    wide(range(KC // 2))
                if has(s, -LAG):
                    n = slot(r, -LAG)
                    if s == LAG:
                        pe.wait_ge(b2_lo_made, 1)
                    pe.wait_ge(ht_lo_made, done - LAG + 1)
                    for l, w, stop in ((ht_hi, b2_hi, False), (ht_hi, b2_lo, False), (ht_lo, b2_hi, True)):
                        nc.tensor.matmul(pair[n][0][:, HEAD:HALF], l[:, :], w[:, 0:Y0],
                                         start=False, stop=stop, skip_group_check=True)
                        lora = nc.tensor.matmul(pair[n][1][:, 0:HALF], l[:, :], w[:, Y0:D],
                                                start=False, stop=stop, skip_group_check=True)
                    lora.then_inc(y_summed, 1)
                if has(s, 0):
                    wide(range(KC // 2, KC))
                    last[0].then_inc(head_ready, 1)
                    last[1].then_inc(wide_done, 1)
                if has(s, -1):
                    pe.wait_ge(h_gated_made, done)
                    nc.tensor.transpose(p_ht[:, 0:P], h_gated[:, :], ident[:, :]).then_inc(ht_turned, 1)

            steps(pe, step)


_INS = ['x', 'itok_B_0_7', 'L0_cond_W', 'L0_cond_Wr', 'L0_cond_A', 'L0_cond_B', 'L0_ffn_sign', 'L0_ffn_scale']


def kernel(**inputs):
    import numpy as _np
    import concourse.bacc as _bacc
    from concourse import mybir as _mybir
    from concourse.bass_utils import run_bass_kernel_spmd as _run

    nc = _bacc.Bacc("TRN2", target_bir_lowering=False, num_devices=1)
    arrays, args = {}, []
    for name in _INS:
        a = _np.ascontiguousarray(inputs[name])
        if a.ndim == 0:
            a = a.reshape(1)
        arrays[f"in_{name}"] = a
        args.append(nc.dram_tensor(f"in_{name}", a.shape, _mybir.dt.from_np(a.dtype), kind="ExternalInput").ap())
    x = inputs['x']
    args.append(nc.dram_tensor("out", x.shape, _mybir.dt.from_np(_np.dtype("float32")), kind="ExternalOutput").ap())
    adaln_ffn_kernel(nc, *args)
    r = _run(nc, [arrays], core_ids=[0])
    return r.results[0]["out"]
```

```python
import concourse.bass as bass
from concourse import mybir
from contextlib import ExitStack

FP32 = mybir.dt.float32
BF16 = mybir.dt.bfloat16
FP32R = mybir.dt.float32r
INT32 = mybir.dt.int32
UINT32 = mybir.dt.uint32
ALU = mybir.AluOpType
ACT = mybir.ActivationFunctionType

P = 128
Q = 32
LANG_BIAS = 5.0
SCALING = 32.0 / 16.0


def adaln_ffn_kernel(nc: bass.Bass, x, lang_ids, W, Wr, A, B, sign, scale, out):
    BATCH, TILES, D = x.shape
    O = W.shape[0]
    E, R = A.shape[0], A.shape[1]
    ER = E * R
    NQ = P // Q
    KC = D // P
    OC = O // P
    HEAD = E + ER
    WIDE = HEAD + D
    Y0 = D // 2
    BANKS = ((0, 0, HEAD + Y0), (1, HEAD + Y0, WIDE))
    assert BATCH == P and ER == P and D % (NQ * Q) == 0 and HEAD + Y0 <= 512 and O == KC * P
    WARM_UPS = 18
    S3 = 3

    x_load = x.rearrange("(g b) t (i c) -> i b t g c", b=Q, i=NQ)
    w_load = W.rearrange("(p j) d -> p j d", j=OC)
    sign_load = sign.rearrange("(p j) n -> p j n", j=OC)
    a_load = A.rearrange("e r d -> (e r) d").rearrange("(g b) (i c) -> i b g c", b=Q, i=NQ)
    wr_load = Wr.rearrange("e (i c) -> i e c", i=NQ)
    b_load = B.rearrange("e (p j) r -> p e (j r)", j=OC)

    ctx = ExitStack()
    with ctx:
        def sb(name, shape, dt=FP32):
            return ctx.enter_context(nc.sbuf_tensor(name, shape, dt))

        def sem(name):
            return ctx.enter_context(nc.semaphore(name))

        w_in = sb("w_in", [P, OC, D])
        sign_in = sb("sign_in", [P, OC, D])
        a_in = sb("a_in", [P, NQ, P])
        wr_in = sb("wr_in", [P, P])
        at = sb("at", [P, NQ, KC, Q])
        wrt = sb("wrt", [P, KC, Q])
        b_in = sb("b_in", [P, E, OC * R])
        ids_in = sb("ids_in", [P, 1], INT32)
        scale_in = sb("scale_in", [P, 1])
        w_hi = sb("w_hi", [P, OC, KC, NQ, Q], FP32R)
        w_lo = sb("w_lo", [P, OC, KC, NQ, Q], FP32R)
        sign_hi = sb("sign_hi", [P, OC, D], FP32R)
        sign_lo = sb("sign_lo", [P, OC, D], FP32R)
        b_hi = sb("b_hi", [P, OC, E, R], FP32R)
        b_lo = sb("b_lo", [P, OC, E, R], FP32R)
        wide_hi = sb("wide_hi", [P, KC, WIDE], FP32R)
        wide_lo = sb("wide_lo", [P, KC, WIDE], FP32R)
        m_full = sb("m_full", [P, KC, D])
        b2_hi = sb("b2_hi", [P, D], FP32R)
        b2_lo = sb("b2_lo", [P, D], FP32R)
        warm_words = sb("warm_words", [P, P])
        warm = warm_words[:, :].bitcast(BF16)
        ident = sb("ident", [P, P])
        eye = sb("eye", [P, KC, D])
        expert_no_int = sb("expert_no_int", [P, E], INT32)
        expert_no = sb("expert_no", [P, E])
        lang = sb("lang", [P, 1])
        bias = sb("bias", [P, E])
        sp = sb("sp", [P, 12])
        exp_neg = sb("exp_neg", [P, 1])
        ln_one = sb("ln_one", [P, 1])
        x_in = [sb(f"x_in{n}", [P, NQ, P]) for n in range(S3)]
        xt = [sb(f"xt{n}", [P, NQ, KC, Q]) for n in range(S3)]
        xt_hi = [sb(f"xt_hi{n}", [P, KC, P], FP32R) for n in range(S3)]
        xt_lo = [sb(f"xt_lo{n}", [P, KC, P], FP32R) for n in range(S3)]
        logits = sb("logits", [P, E])
        top = sb("top", [P, 8])
        top_at = sb("top_at", [P, 8], UINT32)
        top_no = sb("top_no", [P, 2])
        e2 = sb("e2", [P, 1])
        denom = sb("denom", [P, 1])
        rdenom = sb("rdenom", [P, 1])
        second = sb("second", [P, E])
        gate = sb("gate", [P, E])
        h_gated = sb("h_gated", [P, ER])
        ht_hi = sb("ht_hi", [ER, P], FP32R)
        ht_lo = sb("ht_lo", [ER, P], FP32R)
        y = [sb(f"y{n}", [P, D]) for n in range(S3)]

        pair = [[ctx.enter_context(nc.psum_tensor(f"pair{n}{k}", [P, 512], FP32)) for k in range(2)]
                for n in range(S3)]
        p_ht = ctx.enter_context(nc.psum_tensor("p_ht", [P, 512], FP32))
        p_b2 = ctx.enter_context(nc.psum_tensor("p_b2", [P, 512], FP32))
        p_m = [pair[1][0], pair[1][1], pair[2][0], pair[2][1]]

        a_loaded = sem("a_loaded")
        wr_loaded = sem("wr_loaded")
        w_loaded = [sem(f"w_loaded{j}") for j in range(OC)]
        sign_loaded = [sem(f"sign_loaded{j}") for j in range(OC)]
        b_loaded = sem("b_loaded")
        scale_loaded = sem("scale_loaded")
        ids_loaded = sem("ids_loaded")
        warm_zeroed = sem("warm_zeroed")
        zeroed = sem("zeroed")
        ident_made = sem("ident_made")
        eye_made = sem("eye_made")
        experts_numbered = sem("experts_numbered")
        vec_done = sem("vec_done")
        exp_neg_made = sem("exp_neg_made")
        neg_abs_made = sem("neg_abs_made")
        ln_one_made = sem("ln_one_made")
        softplus_made = sem("softplus_made")
        wr_zeroed = sem("wr_zeroed")
        head_turned = sem("head_turned")
        head_hi_made = sem("head_hi_made")
        head_lo_made = sem("head_lo_made")
        w_hi_made = sem("w_hi_made")
        sign_hi_made = sem("sign_hi_made")
        w_lo_made = sem("w_lo_made")
        sign_lo_made = sem("sign_lo_made")
        b_hi_made = sem("b_hi_made")
        b_lo_made = sem("b_lo_made")
        m_summed = sem("m_summed")
        m_full_made = sem("m_full_made")
        m_hi_made = sem("m_hi_made")
        m_lo_even_made = sem("m_lo_even_made")
        m_lo_odd_made = sem("m_lo_odd_made")
        b2_summed = sem("b2_summed")
        b2_hi_made = sem("b2_hi_made")
        b2_lo_made = sem("b2_lo_made")
        x_loaded = [sem(f"x_loaded{n}") for n in range(S3)]
        y_stored = [sem(f"y_stored{n}") for n in range(S3)]
        xt_made = sem("xt_made")
        xt_hi_made = sem("xt_hi_made")
        xt_lo_made = sem("xt_lo_made")
        head_ready = sem("head_ready")
        wide_done = sem("wide_done")
        logits_made = sem("logits_made")
        top_made = sem("top_made")
        top_at_made = sem("top_at_made")
        top_no_made = sem("top_no_made")
        e2_made = sem("e2_made")
        denom_made = sem("denom_made")
        rdenom_made = sem("rdenom_made")
        second_made = sem("second_made")
        gate_made = sem("gate_made")
        h_gated_made = sem("h_gated_made")
        ht_turned = sem("ht_turned")
        ht_hi_made = sem("ht_hi_made")
        ht_lo_made = sem("ht_lo_made")
        y_summed = sem("y_summed")
        y_copied = sem("y_copied")
        last_summed = sem("last_summed")
        last_copied = sem("last_copied")
        last_stored = sem("last_stored")

        block = ctx.enter_context(nc.Block())

        def slot(r, d=0):
            return (r + d) % S3

        def turn(q, r, d=0):
            return q + (r + d) // S3

        LEAD = 2
        LAG = 2
        FIRST = LAG + S3
        LOOPS = (TILES - LEAD - FIRST) // S3
        AFTER = FIRST + S3 * LOOPS

        def steps(eng, step, end=TILES + LAG):
            for s in range(FIRST):
                step(s // S3, s % S3, s)
            with eng.Fori(1, 1 + LOOPS) as q:
                for r in range(FIRST - S3, FIRST):
                    step(q, r, None)
            for s in range(AFTER, end):
                step(s // S3, s % S3, s)

        def has(s, d):
            return s is None or 0 <= s + d < TILES

        @block.sync
        def _(sp_eng):
            def load(q, r, t):
                for i in range(NQ):
                    sp_eng.dma_start(x_in[r % S3][Q * i:Q * i + Q, :, :], x_load[i, :, t, :, :])\
                        .then_inc(x_loaded[r % S3], 16)

            def store(q, r, d):
                sp_eng.wait_ge(y_copied, S3 * q + r + d + 1)
                sp_eng.dma_start(out[:, S3 * q + r + d, :], y[slot(r, d)][:, :])\
                    .then_inc(y_stored[slot(r, d)], 16)

            def store_last():
                n = (TILES - 1) % S3
                sp_eng.wait_ge(last_copied, 1)
                sp_eng.dma_start(out[:, TILES - 1, 0:Y0], y[n][:, 0:Y0]).then_inc(last_stored, 16)
                sp_eng.wait_ge(y_copied, TILES)
                sp_eng.dma_start(out[:, TILES - 1, Y0:D], y[n][:, Y0:D]).then_inc(y_stored[n], 16)

            for j in range(OC):
                sp_eng.dma_start(w_in[:, j, :], w_load[:, j, :]).then_inc(w_loaded[j], 16)
                sp_eng.dma_start(sign_in[:, j, :], sign_load[:, j, :]).then_inc(sign_loaded[j], 16)
            load(0, 0, 0)
            for i in range(NQ):
                sp_eng.dma_start(a_in[Q * i:Q * i + Q, :, :], a_load[i, :, :, :]).then_inc(a_loaded, 16)
            sp_eng.wait_ge(wr_zeroed, 1)
            for i in range(NQ):
                sp_eng.dma_start(wr_in[Q * i:Q * i + E, :], wr_load[i, :, :]).then_inc(wr_loaded, 16)
            sp_eng.dma_start(b_in[:, :, :], b_load).then_inc(b_loaded, 16)
            for t in range(1, S3):
                load(0, t, t)

            def turnover(q, r, s):
                if s is None or s + S3 < TILES:
                    sp_eng.wait_ge(xt_made, S3 * q + r + 1)
                    load(q, r, S3 * q + r + S3)
                if s is None or s >= LAG + LEAD:
                    store(q, r, -LAG - LEAD)

            for s in range(LAG + LEAD):
                turnover(s // S3, s % S3, s)
            loops = (TILES - S3 - LAG - LEAD) // S3
            with sp_eng.Fori(1, 1 + loops) as q:
                for r in range(LAG + LEAD - S3, LAG + LEAD):
                    turnover(q, r, None)
            for s in range(LAG + LEAD + S3 * loops, TILES + LAG + LEAD - 1):
                turnover(s // S3, s % S3, s)
            store_last()
            sp_eng.wait_ge(last_stored, 16)
            for n in range(S3):
                sp_eng.wait_ge(y_stored[n], 16 * len(range(n, TILES, S3)))

        @block.gpsimd
        def _(pool):
            pool.dma_start(scale_in[:, :], scale.partition_broadcast(P)).then_inc(scale_loaded, 16)
            pool.dma_start(ids_in[:, :], lang_ids.rearrange("(p a) -> p a", a=1)).then_inc(ids_loaded, 16)
            nc.gpsimd.memset(wr_in[:, :], 0.0).then_inc(wr_zeroed, 1)
            nc.gpsimd.memset(ident[:, :], 0.0).then_inc(zeroed, 1)
            nc.gpsimd.memset(eye[:, :, :], 0.0).then_inc(zeroed, 1)
            nc.gpsimd.iota(expert_no_int[:, :], [[1, E]], base=0, channel_multiplier=0)\
                .then_inc(experts_numbered, 1)
            pool.wait_ge(zeroed, 2)
            nc.gpsimd.affine_select(out=ident[:, :], in_=ident[:, :], compare_op=ALU.not_equal, fill=1.0,
                                    base=0, pattern=[[-1, P]], channel_multiplier=1).then_inc(ident_made, 1)
            for j in range(KC):
                part = eye[:, j, :].rearrange("p (i k a) -> p i k a", i=NQ, k=KC)[:, :, j, :]
                nc.gpsimd.affine_select(out=part, in_=part, compare_op=ALU.not_equal, fill=1.0, base=0,
                                        pattern=[[-Q, NQ], [-1, Q]], channel_multiplier=1)\
                    .then_inc(eye_made, 1)
            for j in range(OC):
                pool.wait_ge(sign_hi_made, j + 1)
                nc.gpsimd.tensor_tensor(sign_lo[:, j, :], sign_in[:, j, :], sign_hi[:, j, :].bitcast(FP32),
                                        ALU.subtract).then_inc(sign_lo_made, 1)

            def low_x(q, r, d):
                pool.wait_ge(xt_hi_made, S3 * q + r + d + 1)
                n = slot(r, d)
                nc.gpsimd.tensor_tensor(xt_lo[n][:, :, :].rearrange("p j (g b) -> p g j b", g=NQ),
                                        xt[n][:, :, :, :],
                                        xt_hi[n][:, :, :].bitcast(FP32).rearrange("p j (g b) -> p g j b", g=NQ),
                                        ALU.subtract).then_inc(xt_lo_made, 1)

            for t in range(LEAD):
                low_x(0, t, 0)
            for k in range(1, KC, 2):
                pool.wait_ge(m_hi_made, k + 1)
                nc.gpsimd.tensor_tensor(wide_lo[:, k, HEAD:WIDE], m_full[:, k, :],
                                        wide_hi[:, k, HEAD:WIDE].bitcast(FP32), ALU.subtract)\
                    .then_inc(m_lo_odd_made, 1)

            def step(q, r, s):
                if has(s, LEAD):
                    low_x(q, r, LEAD)

            steps(pool, step)

        @block.scalar
        def _(act):
            for j in range(OC):
                act.wait_ge(w_loaded[j], 16)
                nc.scalar.activation(w_hi[:, j, :, :, :],
                                     w_in[:, j, :].rearrange("p (i k a) -> p k i a", i=NQ, k=KC),
                                     ACT.Copy).then_inc(w_hi_made, 1)
            act.wait_ge(neg_abs_made, 1)
            nc.scalar.activation(exp_neg[:, :], sp[:, 1:2], ACT.Exp).then_inc(exp_neg_made, 1)
            act.wait_ge(exp_neg_made, 1)
            nc.scalar.activation(ln_one[:, :], exp_neg[:, :], ACT.Ln, bias=1.0).then_inc(ln_one_made, 1)
            def high_x(q, r, d, first=False):
                n = slot(r, d)
                act.wait_ge(xt_made, S3 * q + r + d + 1)
                if not first:
                    act.wait_ge(wide_done, S3 * q + r + d + 1 - S3)
                nc.scalar.activation(xt_hi[n][:, :, :].rearrange("p j (g b) -> p g j b", g=NQ),
                                     xt[n][:, :, :, :], ACT.Copy).then_inc(xt_hi_made, 1)

            high_x(0, 0, 0, first=True)
            act.wait_ge(head_turned, 1)
            nc.scalar.activation(wide_hi[:, :, E:HEAD].rearrange("p j (g b) -> p g j b", g=NQ), at[:, :, :, :],
                                 ACT.Copy).then_inc(head_hi_made, 1)
            act.wait_ge(head_turned, 2)
            nc.scalar.activation(wide_hi[:, :, 0:E], wrt[:, :, 0:E], ACT.Copy).then_inc(head_hi_made, 1)
            act.wait_ge(b_loaded, 16)
            nc.scalar.activation(b_hi[:, :, :, :], b_in[:, :, :].rearrange("p e (j r) -> p j e r", j=OC),
                                 ACT.Copy).then_inc(b_hi_made, 1)
            for t in range(1, LEAD):
                high_x(0, t, 0, first=True)
            for k in range(KC):
                act.wait_ge(m_full_made, k + 1)
                nc.scalar.activation(wide_hi[:, k, HEAD:WIDE], m_full[:, k, :], ACT.Copy).then_inc(m_hi_made, 1)
            act.wait_ge(softplus_made, 1)
            act.wait_ge(b2_summed, 1)
            nc.scalar.activation(b2_hi[:, :], p_b2[:, :], ACT.Copy, scale=sp[:, 11:12]).then_inc(b2_hi_made, 1)

            def step(q, r, s):
                if has(s, -LAG):
                    act.wait_ge(ht_turned, S3 * q + r - LAG + 1)
                    nc.scalar.activation(ht_hi[:, :], p_ht[:, 0:P], ACT.Copy).then_inc(ht_hi_made, 1)
                if has(s, -1):
                    act.wait_ge(top_made, S3 * q + r)
                    nc.scalar.activation(e2[:, :], top[:, 0:1], ACT.Exp, bias=top[:, 1:2], scale=-1.0)\
                        .then_inc(e2_made, 1)
                if has(s, -LAG):
                    n = slot(r, -LAG)
                    act.wait_ge(y_summed, S3 * q + r - LAG + 1)
                    if s is None or s - LAG >= S3:
                        act.wait_ge(y_stored[n], 16 * turn(q, r, -LAG))
                    if s != TILES - 1 + LAG:
                        nc.scalar.activation(y[n][:, 0:Y0], pair[n][0][:, HEAD:HEAD + Y0], ACT.Copy)
                    nc.scalar.activation(y[n][:, Y0:D], pair[n][1][:, 0:D - Y0], ACT.Copy).then_inc(y_copied, 1)
                if has(s, LEAD):
                    high_x(q, r, LEAD, first=(s is not None and s + LEAD < S3))

            steps(act, step)

        @block.vector
        def _(dve):
            chain = [0]

            def link(ins):
                chain[0] += 1
                ins.then_inc(vec_done, 1)
                dve.wait_ge(vec_done, chain[0])

            nc.vector.memset(warm_words[:, :], 0.0).then_inc(warm_zeroed, 1)
            for j in range(OC):
                dve.wait_ge(sign_loaded[j], 16)
                nc.vector.tensor_copy(sign_hi[:, j, :], sign_in[:, j, :]).then_inc(sign_hi_made, 1)
                dve.wait_ge(w_hi_made, j + 1)
                nc.vector.tensor_tensor(w_lo[:, j, :, :, :],
                                        w_in[:, j, :].rearrange("p (i k a) -> p k i a", i=NQ, k=KC),
                                        w_hi[:, j, :, :, :].bitcast(FP32), ALU.subtract).then_inc(w_lo_made, 1)
            dve.wait_ge(scale_loaded, 16)
            link(nc.vector.tensor_scalar(sp[:, 0:1], scale_in[:, :], -1.0, None, ALU.mult))
            nc.vector.tensor_tensor(sp[:, 1:2], sp[:, 0:1], scale_in[:, :], ALU.min).then_inc(neg_abs_made, 1)
            dve.wait_ge(ids_loaded, 16)
            dve.wait_ge(experts_numbered, 1)
            nc.vector.tensor_copy(expert_no[:, :], expert_no_int[:, :])
            link(nc.vector.tensor_copy(lang[:, :], ids_in[:, :]))
            link(nc.vector.tensor_scalar(bias[:, :], expert_no[:, :], lang[:, 0:1], LANG_BIAS,
                                         ALU.is_equal, ALU.mult))

            def turn_x(q, r, d, first=False):
                n = slot(r, d)
                dve.wait_ge(x_loaded[n], 16 * NQ * (turn(q, r, d) + 1))
                if not first:
                    dve.wait_ge(xt_lo_made, S3 * q + r + d + 1 - S3)
                nc.vector.transpose(xt[n][:, :, :, :].rearrange("p g j b -> p (g j b)"),
                                    x_in[n][:, :, :].rearrange("p g c -> p (g c)")).then_inc(xt_made, 1)

            turn_x(0, 0, 0, first=True)
            dve.wait_ge(a_loaded, 16 * NQ)
            nc.vector.transpose(at[:, :, :, :].rearrange("p g j b -> p (g j b)"),
                                a_in[:, :, :].rearrange("p g c -> p (g c)")).then_inc(head_turned, 1)
            dve.wait_ge(exp_neg_made, 1)
            link(nc.vector.tensor_scalar(sp[:, 2:3], exp_neg[:, :], 1.0, None, ALU.add))
            link(nc.vector.tensor_scalar(sp[:, 3:4], sp[:, 2:3], -1.0, None, ALU.add))
            link(nc.vector.tensor_scalar(sp[:, 4:5], sp[:, 3:4], 0.0, None, ALU.is_equal))
            link(nc.vector.tensor_tensor(sp[:, 5:6], sp[:, 3:4], sp[:, 4:5], ALU.add))
            link(nc.vector.reciprocal(sp[:, 6:7], sp[:, 5:6]))
            dve.wait_ge(ln_one_made, 1)
            link(nc.vector.tensor_tensor(sp[:, 7:8], ln_one[:, :], sp[:, 4:5], ALU.add))
            link(nc.vector.tensor_tensor(sp[:, 8:9], sp[:, 7:8], sp[:, 6:7], ALU.mult))
            link(nc.vector.tensor_tensor(sp[:, 9:10], sp[:, 8:9], exp_neg[:, :], ALU.mult))
            link(nc.vector.scalar_tensor_tensor(sp[:, 10:11], scale_in[:, :], 0.0, sp[:, 9:10], ALU.max, ALU.add))
            nc.vector.tensor_scalar(sp[:, 11:12], sp[:, 10:11], SCALING, None, ALU.mult).then_inc(softplus_made, 1)
            softplus = sp[:, 10:11]
            dve.wait_ge(wr_loaded, 16 * NQ)
            nc.vector.transpose(wrt[:, :, :].rearrange("p j b -> p (j b)"), wr_in[:, :]).then_inc(head_turned, 1)
            dve.wait_ge(head_hi_made, 2)
            nc.vector.tensor_tensor(wide_lo[:, :, 0:E], wrt[:, :, 0:E], wide_hi[:, :, 0:E].bitcast(FP32),
                                    ALU.subtract)
            nc.vector.tensor_tensor(wide_lo[:, :, E:HEAD].rearrange("p j (g b) -> p g j b", g=NQ), at[:, :, :, :],
                                    wide_hi[:, :, E:HEAD].bitcast(FP32).rearrange("p j (g b) -> p g j b", g=NQ),
                                    ALU.subtract).then_inc(head_lo_made, 1)
            dve.wait_ge(b_hi_made, 1)
            nc.vector.tensor_tensor(b_lo[:, :, :, :], b_in[:, :, :].rearrange("p e (j r) -> p j e r", j=OC),
                                    b_hi[:, :, :, :].bitcast(FP32), ALU.subtract).then_inc(b_lo_made, 1)
            for t in range(1, LEAD):
                turn_x(0, t, 0, first=True)
            dve.wait_ge(eye_made, KC)
            for k in range(KC):
                dve.wait_ge(m_summed, k + 1)
                nc.vector.scalar_tensor_tensor(m_full[:, k, :], p_m[k][:, :], softplus, eye[:, k, :],
                                               ALU.mult, ALU.add).then_inc(m_full_made, 1)
                if k % 2:
                    dve.wait_ge(m_hi_made, k)
                    nc.vector.tensor_tensor(wide_lo[:, k - 1, HEAD:WIDE], m_full[:, k - 1, :],
                                            wide_hi[:, k - 1, HEAD:WIDE].bitcast(FP32),
                                            ALU.subtract).then_inc(m_lo_even_made, 1)
            dve.wait_ge(b2_hi_made, 1)
            nc.vector.scalar_tensor_tensor(b2_lo[:, :], p_b2[:, :], sp[:, 11:12], b2_hi[:, :].bitcast(FP32),
                                           ALU.mult, ALU.subtract).then_inc(b2_lo_made, 1)

            def low_h(done):
                dve.wait_ge(ht_hi_made, done - LAG + 1)
                nc.vector.tensor_tensor(ht_lo[:, :], p_ht[:, 0:P], ht_hi[:, :].bitcast(FP32), ALU.subtract)\
                    .then_inc(ht_lo_made, 1)

            def step(q, r, s):
                done = S3 * q + r
                n = slot(r, -1)
                if has(s, -1):
                    dve.wait_ge(head_ready, done)
                    nc.vector.tensor_tensor(logits[:, :], pair[n][0][:, 0:E], bias[:, :], ALU.add)\
                        .then_inc(logits_made, 1)
                    dve.wait_ge(logits_made, done)
                hurry = s is not None and s >= TILES - 1
                if has(s, -LAG) and not hurry:
                    low_h(done)
                if has(s, -1):
                    nc.vector.max(top[:, :], logits[:, :]).then_inc(top_made, 1)
                    dve.wait_ge(top_made, done)
                if has(s, LEAD):
                    turn_x(q, r, LEAD, first=(s is not None and s + LEAD < S3))
                if has(s, -1):
                    nc.vector.max_index(top_at[:, :], top[:, :], logits[:, :]).then_inc(top_at_made, 1)
                if has(s, -LAG) and hurry:
                    low_h(done)
                if has(s, -1):
                    dve.wait_ge(top_at_made, done)
                    nc.vector.tensor_copy(top_no[:, :], top_at[:, 0:2]).then_inc(top_no_made, 1)
                    dve.wait_ge(e2_made, done)
                    nc.vector.tensor_scalar(denom[:, :], e2[:, :], 1.0, None, ALU.add).then_inc(denom_made, 1)
                    dve.wait_ge(top_no_made, done)
                    nc.vector.tensor_scalar(second[:, :], expert_no[:, :], top_no[:, 1:2], e2[:, 0:1],
                                            ALU.is_equal, ALU.mult).then_inc(second_made, 1)
                    dve.wait_ge(denom_made, done)
                    nc.vector.reciprocal(rdenom[:, :], denom[:, :]).then_inc(rdenom_made, 1)
                    dve.wait_ge(second_made, done)
                    nc.vector.scalar_tensor_tensor(gate[:, :], expert_no[:, :], top_no[:, 0:1], second[:, :],
                                                   ALU.is_equal, ALU.add).then_inc(gate_made, 1)
                    dve.wait_ge(rdenom_made, done)
                    dve.wait_ge(gate_made, done)
                    nc.vector.scalar_tensor_tensor(
                        h_gated[:, :].rearrange("p (e r) -> p e r", e=E),
                        pair[n][0][:, E:HEAD].rearrange("p (e r) -> p e r", e=E), rdenom[:, 0:1],
                        gate[:, :].unsqueeze(2).to_broadcast([P, E, R]), ALU.mult, ALU.mult)\
                        .then_inc(h_gated_made, 1)
                if s == TILES - 1 + LAG:
                    n = (TILES - 1) % S3
                    dve.wait_ge(last_summed, 1)
                    dve.wait_ge(y_stored[n], 16 * turn(q, r, -LAG))
                    nc.vector.tensor_copy(y[n][:, 0:Y0], pair[n][0][:, HEAD:HEAD + Y0]).then_inc(last_copied, 1)

            steps(dve, step)

        @block.tensor
        def _(pe):
            def three(out_ap, l_hi, l_lo, r_hi, r_lo, start, stop):
                nc.tensor.matmul(out_ap, l_hi, r_hi, start=start, stop=False, skip_group_check=True)
                nc.tensor.matmul(out_ap, l_hi, r_lo, start=False, stop=False, skip_group_check=True)
                return nc.tensor.matmul(out_ap, l_lo, r_hi, start=False, stop=stop, skip_group_check=True)

            pe.wait_ge(warm_zeroed, 1)
            for _ in range(WARM_UPS):
                nc.tensor.matmul(p_b2[:, 0:2 * P], warm[:, 0:P], warm[:, :], start=True, stop=True)

            w_cols = lambda part, j, k: part[:, j, k, :, :].rearrange("p i a -> p (i a)")
            for j in range(OC - 1):
                pe.wait_ge(w_hi_made, j + 1)
                pe.wait_ge(sign_hi_made, j + 1)
                for k in range(KC):
                    nc.tensor.matmul(p_m[k][:, :], w_cols(w_hi, j, k), sign_hi[:, j, :], start=(j == 0), stop=False,
                                     skip_group_check=True)
                pe.wait_ge(w_lo_made, j + 1)
                for k in range(KC):
                    nc.tensor.matmul(p_m[k][:, :], w_cols(w_lo, j, k), sign_hi[:, j, :], start=False, stop=False,
                                     skip_group_check=True)
                pe.wait_ge(sign_lo_made, j + 1)
                for k in range(KC):
                    nc.tensor.matmul(p_m[k][:, :], w_cols(w_hi, j, k), sign_lo[:, j, :], start=False, stop=False,
                                     skip_group_check=True)
            pe.wait_ge(w_lo_made, OC)
            pe.wait_ge(sign_lo_made, OC)
            for k in range(KC):
                three(p_m[k][:, :], w_cols(w_hi, OC - 1, k), w_cols(w_lo, OC - 1, k),
                      sign_hi[:, OC - 1, :], sign_lo[:, OC - 1, :], False, True).then_inc(m_summed, 1)
            pe.wait_ge(b_lo_made, 1)
            for j in range(OC):
                last = three(p_b2[:, :], b_hi[:, j, :, :].rearrange("p e r -> p (e r)"),
                             b_lo[:, j, :, :].rearrange("p e r -> p (e r)"),
                             sign_hi[:, j, :], sign_lo[:, j, :], j == 0, j == OC - 1)
            last.then_inc(b2_summed, 1)

            def wide(r, chunks, cols, opens=False, signals=False):
                n = slot(r)
                for k in chunks:
                    for l, w in ((xt_hi[n], wide_hi), (xt_hi[n], wide_lo), (xt_lo[n], wide_hi)):
                        for bank, lo, hi in cols:
                            at0 = lo - BANKS[bank][1]
                            last = nc.tensor.matmul(pair[n][bank][:, at0:at0 + hi - lo], l[:, k, :], w[:, k, lo:hi],
                                                    start=(opens and k == 0 and l is xt_hi[n] and w is wide_hi),
                                                    stop=False, skip_group_check=True)
                            if signals and k == KC - 1 and l is xt_lo[n]:
                                last.then_inc((head_ready, wide_done)[bank], 1)
                return last

            def m_there(s, k):
                if s == 0:
                    pe.wait_ge((m_lo_even_made, m_lo_odd_made)[k % 2], k // 2 + 1)

            def lora(n, banks):
                for l, w, stop in ((ht_hi, b2_hi, False), (ht_hi, b2_lo, False), (ht_lo, b2_hi, True)):
                    for bank in banks:
                        o = pair[n][bank][:, (HEAD, 0)[bank]:(HEAD + Y0, D - Y0)[bank]]
                        last = nc.tensor.matmul(o, l[:, :], w[:, (0, Y0)[bank]:(Y0, D)[bank]],
                                                start=False, stop=stop, skip_group_check=True)
                return last

            def turn_h(done):
                pe.wait_ge(h_gated_made, done)
                nc.tensor.transpose(p_ht[:, 0:P], h_gated[:, :], ident[:, :]).then_inc(ht_turned, 1)

            def step(q, r, s):
                done = S3 * q + r
                if has(s, 0):
                    pe.wait_ge(xt_lo_made, done + 1)
                    if s is None or s >= S3:
                        pe.wait_ge(y_copied, done - S3 + 1)
                    for k in range(KC // 2):
                        m_there(s, k)
                        wide(r, [k], BANKS, opens=True)
                if has(s, -LAG):
                    if s == LAG:
                        pe.wait_ge(b2_lo_made, 1)
                    pe.wait_ge(ht_lo_made, done - LAG + 1)
                    lora(slot(r, -LAG), (0, 1)).then_inc(y_summed, 1)
                if has(s, 0):
                    for k in range(KC // 2, KC):
                        m_there(s, k)
                        wide(r, [k], BANKS, signals=True)
                if has(s, -1):
                    turn_h(done)

            def finish(s):
                r, n = s % S3, s % S3
                everything = range(KC)
                pe.wait_ge(xt_lo_made, s + 1)
                pe.wait_ge(y_copied, s - S3 + 1)
                wide(r, everything, ((0, 0, HEAD),), opens=True).then_inc(head_ready, 1)
                pe.wait_ge(ht_lo_made, s - LAG + 1)
                lora(slot(r, -LAG), (0, 1)).then_inc(y_summed, 1)
                wide(r, range(KC // 2), (BANKS[1],), opens=True)
                turn_h(s)
                wide(r, range(KC // 2, KC), (BANKS[1],))
                pe.wait_ge(ht_lo_made, s)
                lora(slot(r, -1), (0, 1)).then_inc(y_summed, 1)
                turn_h(s + 1)
                wide(r, everything, ((0, HEAD, HEAD + Y0),))
                pe.wait_ge(ht_lo_made, s + 1)
                lora(n, (0,)).then_inc(last_summed, 1)
                lora(n, (1,)).then_inc(y_summed, 1)

            pe.wait_ge(head_lo_made, 1)
            pe.wait_ge(ident_made, 1)
            steps(pe, step, TILES - 1)
            finish(TILES - 1)


_INS = ['x', 'itok_B_0_7', 'L0_cond_W', 'L0_cond_Wr', 'L0_cond_A', 'L0_cond_B', 'L0_ffn_sign', 'L0_ffn_scale']


def kernel(**inputs):
    import numpy as _np
    import concourse.bacc as _bacc
    from concourse import mybir as _mybir
    from concourse.bass_utils import run_bass_kernel_spmd as _run

    nc = _bacc.Bacc("TRN2", target_bir_lowering=False, num_devices=1)
    arrays, args = {}, []
    for name in _INS:
        a = _np.ascontiguousarray(inputs[name])
        if a.ndim == 0:
            a = a.reshape(1)
        arrays[f"in_{name}"] = a
        args.append(nc.dram_tensor(f"in_{name}", a.shape, _mybir.dt.from_np(a.dtype), kind="ExternalInput").ap())
    x = inputs['x']
    args.append(nc.dram_tensor("out", x.shape, _mybir.dt.from_np(_np.dtype("float32")), kind="ExternalOutput").ap())
    adaln_ffn_kernel(nc, *args)
    r = _run(nc, [arrays], core_ids=[0])
    return r.results[0]["out"]
```
